# Optimizing a Trainium2 kernel written in Bass

```python
import numpy as np
import jax
import jax.numpy as jnp

def _softmax(x, axis=-1):
    return jax.nn.softmax(x, axis=axis)

def _gelu(x):
    return jax.nn.gelu(x, approximate=True)

def _silu(x):
    return jax.nn.silu(x)

def _sigmoid(x):
    return jax.nn.sigmoid(x)

def _layernorm(x, axis=-1, eps=1e-05):
    m = jnp.mean(x, axis=axis, keepdims=True)
    v = jnp.var(x, axis=axis, keepdims=True)
    return (x - m) / jnp.sqrt(v + eps)

def _scatter_add(tgt, idx, src, axis=0):
    return tgt.at[idx].add(src)

def _segment_sum(src, seg, n):
    return jax.ops.segment_sum(src, seg, n)
kernel_name = 'mk_dlrm_tower_d1_rec_r8_5b6c12'

def setup_inputs(seed: int=0):
    np.random.seed(seed)
    _w = jnp.asarray

    def _rec_inputs():
        import jax
        import jax.numpy as jnp
        _tk = jax.random.key(seed)
        ids = jnp.stack([jax.random.randint(jax.random.fold_in(_tk, 200 + f), (512,), 0, v, jnp.int32) for f, v in enumerate([1250, 1000, 125000, 1250, 1000, 1000, 12500, 12500, 1000, 1250, 12500, 12500, 12500, 1250, 12500, 12500, 1000, 12500, 1000, 1000, 1000, 1250, 1000, 1250, 1000, 1000, 1250])], axis=1)
        tbl_0 = 0.05 * jax.random.normal(jax.random.fold_in(_tk, 500 + 0), (1250, 128), jnp.float32)
        tbl_1 = 0.05 * jax.random.normal(jax.random.fold_in(_tk, 500 + 1), (1000, 128), jnp.float32)
        tbl_2 = 0.05 * jax.random.normal(jax.random.fold_in(_tk, 500 + 2), (125000, 128), jnp.float32)
        tbl_3 = 0.05 * jax.random.normal(jax.random.fold_in(_tk, 500 + 3), (1250, 128), jnp.float32)
        tbl_4 = 0.05 * jax.random.normal(jax.random.fold_in(_tk, 500 + 4), (1000, 128), jnp.float32)
        tbl_5 = 0.05 * jax.random.normal(jax.random.fold_in(_tk, 500 + 5), (1000, 128), jnp.float32)
        tbl_6 = 0.05 * jax.random.normal(jax.random.fold_in(_tk, 500 + 6), (12500, 128), jnp.float32)
        tbl_7 = 0.05 * jax.random.normal(jax.random.fold_in(_tk, 500 + 7), (12500, 128), jnp.float32)
        tbl_8 = 0.05 * jax.random.normal(jax.random.fold_in(_tk, 500 + 8), (1000, 128), jnp.float32)
        tbl_9 = 0.05 * jax.random.normal(jax.random.fold_in(_tk, 500 + 9), (1250, 128), jnp.float32)
        tbl_10 = 0.05 * jax.random.normal(jax.random.fold_in(_tk, 500 + 10), (12500, 128), jnp.float32)
        tbl_11 = 0.05 * jax.random.normal(jax.random.fold_in(_tk, 500 + 11), (12500, 128), jnp.float32)
        tbl_12 = 0.05 * jax.random.normal(jax.random.fold_in(_tk, 500 + 12), (12500, 128), jnp.float32)
        tbl_13 = 0.05 * jax.random.normal(jax.random.fold_in(_tk, 500 + 13), (1250, 128), jnp.float32)
        tbl_14 = 0.05 * jax.random.normal(jax.random.fold_in(_tk, 500 + 14), (12500, 128), jnp.float32)
        tbl_15 = 0.05 * jax.random.normal(jax.random.fold_in(_tk, 500 + 15), (12500, 128), jnp.float32)
        tbl_16 = 0.05 * jax.random.normal(jax.random.fold_in(_tk, 500 + 16), (1000, 128), jnp.float32)
        tbl_17 = 0.05 * jax.random.normal(jax.random.fold_in(_tk, 500 + 17), (12500, 128), jnp.float32)
        tbl_18 = 0.05 * jax.random.normal(jax.random.fold_in(_tk, 500 + 18), (1000, 128), jnp.float32)
        tbl_19 = 0.05 * jax.random.normal(jax.random.fold_in(_tk, 500 + 19), (1000, 128), jnp.float32)
        tbl_20 = 0.05 * jax.random.normal(jax.random.fold_in(_tk, 500 + 20), (1000, 128), jnp.float32)
        tbl_21 = 0.05 * jax.random.normal(jax.random.fold_in(_tk, 500 + 21), (1250, 128), jnp.float32)
        tbl_22 = 0.05 * jax.random.normal(jax.random.fold_in(_tk, 500 + 22), (1000, 128), jnp.float32)
        tbl_23 = 0.05 * jax.random.normal(jax.random.fold_in(_tk, 500 + 23), (1250, 128), jnp.float32)
        tbl_24 = 0.05 * jax.random.normal(jax.random.fold_in(_tk, 500 + 24), (1000, 128), jnp.float32)
        tbl_25 = 0.05 * jax.random.normal(jax.random.fold_in(_tk, 500 + 25), (1000, 128), jnp.float32)
        tbl_26 = 0.05 * jax.random.normal(jax.random.fold_in(_tk, 500 + 26), (1250, 128), jnp.float32)
        _rk = jax.random.fold_in(_tk, 7)
        r_bottom_mlp_out = 4.13588e-05 + 0.999923 * jax.random.normal(jax.random.fold_in(_rk, 101), (512, 128), jnp.float32)
        W_top1 = 0.0405887 * jax.random.normal(jax.random.fold_in(_tk, 801), (607, 512), jnp.float32)
        W_top2 = 0.0441942 * jax.random.normal(jax.random.fold_in(_tk, 802), (512, 256), jnp.float32)
        W_top3 = 0.0625 * jax.random.normal(jax.random.fold_in(_tk, 803), (256, 1), jnp.float32)
        b_top1 = jnp.zeros((512,), jnp.float32)
        b_top2 = jnp.zeros((256,), jnp.float32)
        return (r_bottom_mlp_out, ids, tbl_0, tbl_1, tbl_2, tbl_3, tbl_4, tbl_5, tbl_6, tbl_7, tbl_8, tbl_9, tbl_10, tbl_11, tbl_12, tbl_13, tbl_14, tbl_15, tbl_16, tbl_17, tbl_18, tbl_19, tbl_20, tbl_21, tbl_22, tbl_23, tbl_24, tbl_25, tbl_26, W_top1, b_top1, W_top2, b_top2, W_top3)
    r_bottom_mlp_out, ids, tbl_0, tbl_1, tbl_2, tbl_3, tbl_4, tbl_5, tbl_6, tbl_7, tbl_8, tbl_9, tbl_10, tbl_11, tbl_12, tbl_13, tbl_14, tbl_15, tbl_16, tbl_17, tbl_18, tbl_19, tbl_20, tbl_21, tbl_22, tbl_23, tbl_24, tbl_25, tbl_26, W_top1, b_top1, W_top2, b_top2, W_top3 = _rec_inputs()

    def _L0_rec_setup():
        import jax, jax.numpy as jnp
        import numpy as np
        NUM_FEATURES = 27

        def _tril_indices(F):
            idx = []
            for i in range(F):
                for j in range(i):
                    idx.append(i * F + j)
            return np.asarray(idx, dtype=np.int32)
        TRIL_IDX = _tril_indices(NUM_FEATURES)
        key = jax.random.key(seed)
        k1, k2 = jax.random.split(key)
        B, F, D = (8192, NUM_FEATURES, 128)
        features = jax.random.normal(k1, (B, F, D), dtype=jnp.float32)
        bottom_mlp_out = jax.random.normal(k2, (B, D), dtype=jnp.float32)
        return {'features': features, 'bottom_mlp_out': bottom_mlp_out}
    _L0_rec_all = _L0_rec_setup()
    _L0_rec_in = {k: v for k, v in _L0_rec_all.items() if k in ()}
    del _L0_rec_all
    return {'r_bottom_mlp_out': r_bottom_mlp_out, 'ids': ids, 'tbl_0': tbl_0, 'tbl_1': tbl_1, 'tbl_2': tbl_2, 'tbl_3': tbl_3, 'tbl_4': tbl_4, 'tbl_5': tbl_5, 'tbl_6': tbl_6, 'tbl_7': tbl_7, 'tbl_8': tbl_8, 'tbl_9': tbl_9, 'tbl_10': tbl_10, 'tbl_11': tbl_11, 'tbl_12': tbl_12, 'tbl_13': tbl_13, 'tbl_14': tbl_14, 'tbl_15': tbl_15, 'tbl_16': tbl_16, 'tbl_17': tbl_17, 'tbl_18': tbl_18, 'tbl_19': tbl_19, 'tbl_20': tbl_20, 'tbl_21': tbl_21, 'tbl_22': tbl_22, 'tbl_23': tbl_23, 'tbl_24': tbl_24, 'tbl_25': tbl_25, 'tbl_26': tbl_26, 'W_top1': W_top1, 'b_top1': b_top1, 'W_top2': W_top2, 'b_top2': b_top2, 'W_top3': W_top3}

def reference(r_bottom_mlp_out, ids, tbl_0, tbl_1, tbl_2, tbl_3, tbl_4, tbl_5, tbl_6, tbl_7, tbl_8, tbl_9, tbl_10, tbl_11, tbl_12, tbl_13, tbl_14, tbl_15, tbl_16, tbl_17, tbl_18, tbl_19, tbl_20, tbl_21, tbl_22, tbl_23, tbl_24, tbl_25, tbl_26, W_top1, b_top1, W_top2, b_top2, W_top3):
    import jax
    import jax.numpy as jnp

    def _L0_rec_ref(features, bottom_mlp_out):
        import jax, jax.numpy as jnp
        import numpy as np
        NUM_FEATURES = 27

        def _tril_indices(F):
            idx = []
            for i in range(F):
                for j in range(i):
                    idx.append(i * F + j)
            return np.asarray(idx, dtype=np.int32)
        TRIL_IDX = _tril_indices(NUM_FEATURES)
        B = features.shape[0]
        F = features.shape[1]
        interactions = jnp.einsum('bfd,bgd->bfg', features, features)
        interactions = interactions.reshape(B, F * F)
        x = interactions[:, TRIL_IDX]
        return jnp.concatenate([bottom_mlp_out, x], axis=1)
    e = jnp.stack([tbl_0[ids[:, 0]], tbl_1[ids[:, 1]], tbl_2[ids[:, 2]], tbl_3[ids[:, 3]], tbl_4[ids[:, 4]], tbl_5[ids[:, 5]], tbl_6[ids[:, 6]], tbl_7[ids[:, 7]], tbl_8[ids[:, 8]], tbl_9[ids[:, 9]], tbl_10[ids[:, 10]], tbl_11[ids[:, 11]], tbl_12[ids[:, 12]], tbl_13[ids[:, 13]], tbl_14[ids[:, 14]], tbl_15[ids[:, 15]], tbl_16[ids[:, 16]], tbl_17[ids[:, 17]], tbl_18[ids[:, 18]], tbl_19[ids[:, 19]], tbl_20[ids[:, 20]], tbl_21[ids[:, 21]], tbl_22[ids[:, 22]], tbl_23[ids[:, 23]], tbl_24[ids[:, 24]], tbl_25[ids[:, 25]], tbl_26[ids[:, 26]]], axis=1)
    z = _L0_rec_ref(e, r_bottom_mlp_out)
    z = z.reshape(z.shape[0], -1)
    h = jnp.concatenate([z, r_bottom_mlp_out], axis=1)
    h = jnp.maximum(h @ W_top1 + b_top1, 0.0)
    h = jnp.maximum(h @ W_top2 + b_top2, 0.0)
    y = h @ W_top3
    return y

_drawn_inputs = setup_inputs


def setup_inputs(seed=0):
    import zlib

    import numpy as np

    out = dict(_drawn_inputs(seed))
    spreads = {'b_top1': (0.0, 0.1), 'b_top2': (0.0, 0.1)}
    factors = {'tbl_0': 4.783,
     'tbl_1': 5.112,
     'tbl_2': 4.486,
     'tbl_3': 4.42,
     'tbl_4': 4.721,
     'tbl_5': 4.27,
     'tbl_6': 4.534,
     'tbl_7': 4.045,
     'tbl_8': 4.639,
     'tbl_9': 5.004,
     'tbl_10': 4.352,
     'tbl_11': 4.566,
     'tbl_12': 4.34,
     'tbl_13': 4.433,
     'tbl_14': 4.755,
     'tbl_15': 5.153,
     'tbl_16': 4.65,
     'tbl_17': 5.237,
     'tbl_18': 4.186,
     'tbl_19': 4.202,
     'tbl_20': 4.233,
     'tbl_21': 4.681,
     'tbl_22': 4.585,
     'tbl_23': 4.806,
     'tbl_24': 4.309,
     'tbl_25': 4.735,
     'tbl_26': 4.426}
    for name, (base, spread) in spreads.items():
        noise = np.random.default_rng([zlib.crc32(name.encode()), seed]).standard_normal(out[name].shape)
        drawn = base * np.exp(spread * noise) if base else spread * noise
        out[name] = jnp.asarray(drawn.astype(out[name].dtype))
    for name, factor in factors.items():
        out[name] = (out[name] * factor).astype(out[name].dtype)
    return out
```

```python
import concourse.bass as bass
from concourse import mybir
from contextlib import ExitStack

BATCH, FEATURES, DIM = 512, 27, 128
HIDDEN1, HIDDEN2 = 512, 256
TABLE_ROWS = [1250, 1000, 125000, 1250, 1000, 1000, 12500, 12500, 1000, 1250, 12500, 12500, 12500, 1250,
              12500, 12500, 1000, 12500, 1000, 1000, 1000, 1250, 1000, 1250, 1000, 1000, 1250]
P = 128
TILES = BATCH // P
SLOTS = 2
PAIRS_OF_TILES = TILES // SLOTS

ONE_HOT = 4
SMALL_ROWS = 1000
SMALL_P = 125
SMALL_K = SMALL_ROWS // SMALL_P
SPRAY = SMALL_P // 16 * 16
ONE_HOT_FEATURES = [f for f in range(FEATURES) if TABLE_ROWS[f] == SMALL_ROWS][:ONE_HOT]

ORDER = ONE_HOT_FEATURES + [f for f in range(FEATURES) if f not in ONE_HOT_FEATURES]
BOTTOM = FEATURES
FPC = 4


def cut(entries):
    return [entries[a:a + FPC] for a in range(0, len(entries), FPC)]


CHUNKS = cut(list(range(ONE_HOT))) + cut([BOTTOM] + list(range(ONE_HOT, FEATURES)))
NC = len(CHUNKS)
ENTRIES = FEATURES + 1 - ONE_HOT

QUADRANT = 32
PACK = P // QUADRANT
COLUMNS = FEATURES - 1
GROUPS = -(-COLUMNS // PACK)
FILLED = COLUMNS % PACK * QUADRANT
PPB = 4
NB = P // (PACK * PPB)
BANKS = 2
N1 = HIDDEN1 // P
N2 = HIDDEN2 // P


def dlrm_tower(nc, bottom, ids, small_ids, small_iota, tables, w_pairs, w_bottom, b1, w2, b2, w3, out):
    fp32 = mybir.dt.float32
    u32 = mybir.dt.uint32
    ALU = mybir.AluOpType
    ACT = mybir.ActivationFunctionType

    with ExitStack() as ctx:
        def sb(name, shape, dt=fp32):
            return ctx.enter_context(nc.sbuf_tensor(name, shape, dt))

        def ps(name, shape):
            return ctx.enter_context(nc.psum_tensor(name, shape, fp32))

        def sem(name):
            return ctx.enter_context(nc.semaphore(name))

        ids_sb = sb("ids_sb", [P, TILES * FEATURES], u32)
        small_ids_sb = sb("small_ids_sb", [P, ONE_HOT, BATCH], u32)
        small_iota_sb = sb("small_iota_sb", [P, SMALL_K])
        small = [sb(f"small{x}", [P, SMALL_K, DIM]) for x in range(ONE_HOT)]
        one_hot = sb("one_hot", [P, ONE_HOT * SMALL_K, BATCH])
        rows = [sb(f"rows{k}", [P, ENTRIES, DIM]) for k in range(SLOTS)]
        rowsT = [sb(f"rowsT{k}", [DIM, P, QUADRANT]) for k in range(SLOTS)]
        bottomT = [sb(f"bottomT{k}", [DIM, P]) for k in range(SLOTS)]
        pairs = [sb(f"pairs{k}", [P, GROUPS, P]) for k in range(SLOTS)]
        ident = sb("ident", [P, P])
        wp = sb("wp", [P, GROUPS, HIDDEN1])
        wb = sb("wb", [P, 2, HIDDEN1])
        wb_sum = sb("wb_sum", [P, HIDDEN1])
        w2_sb = sb("w2_sb", [P, N1, HIDDEN2])
        w3_sb = sb("w3_sb", [P, N2])
        b1_sb = sb("b1_sb", [P, N1])
        b2_sb = sb("b2_sb", [P, N2])
        h1 = sb("h1", [P, N1, P])
        h2 = sb("h2", [P, N2, P])
        y_sb = sb("y_sb", [1, BATCH])

        ps_rows = [ps(f"ps_rows{i}", [P, FPC, P]) for i in range(BANKS)]
        ps_prod = [ps(f"ps_prod{i}", [P, BATCH]) for i in range(BANKS)]
        ps_acc = [ps(f"ps_acc{i}", [P, BATCH]) for i in range(N1)]
        Y_BANK = N2

        ids_loaded = sem("ids_loaded")
        small_ids_loaded = sem("small_ids_loaded")
        small_loaded = [sem(f"small_loaded{x}") for x in range(ONE_HOT)]
        weights_loaded = sem("weights_loaded")
        ident_zeroed = sem("ident_zeroed")
        ident_ready = sem("ident_ready")
        wb_summed = sem("wb_summed")
        one_hot_ready = sem("one_hot_ready")
        gathered = [[sem(f"gathered{k}_{c}") for c in range(NC)] for k in range(SLOTS)]
        bottom_loaded = [sem(f"bottom_loaded{k}") for k in range(SLOTS)]
        rows_transposed = sem("rows_transposed")
        rowsT_written = sem("rowsT_written")
        products_done = sem("products_done")
        taken_act = sem("taken_act")
        taken_dve = sem("taken_dve")
        slot_free = [sem(f"slot_free{k}") for k in range(SLOTS)]
        layer1_done = sem("layer1_done")
        layer2_done = sem("layer2_done")
        layer3_done = sem("layer3_done")
        h1_written = sem("h1_written")
        h2_written = sem("h2_written")
        y_written = sem("y_written")
        y_stored = sem("y_stored")

        WEIGHT_LOADS = 6

        def entry(e):
            return e - ONE_HOT

        def take_products(engine_copy, k, b, samples):
            src = ps_prod[b % BANKS][:, 0:PPB * PACK * COLUMNS].rearrange("p (m s g) -> p m s g", m=PPB, s=PACK)
            first = b * PPB * PACK
            dst = pairs[k][:, :, first:first + PPB * PACK].rearrange("p g (m s) -> p m s g", s=PACK)
            last = None
            for s in samples:
                for q in range(PACK):
                    n = -(-(COLUMNS - q) // PACK)
                    last = engine_copy(
                        dst[q * QUADRANT:(q + 1) * QUADRANT, :, s, 0:n],
                        src[s * QUADRANT:(s + 1) * QUADRANT, :, s, q:q + (n - 1) * PACK + 1:PACK])
            return last

        block = ctx.enter_context(nc.Block())

        @block.sync
        def _(sp):
            sp.dma_start(ids_sb[:].rearrange("p (t f) -> p t f", f=FEATURES),
                         ids.rearrange("(t p) f -> p t f", p=P)).then_inc(ids_loaded, 16)
            sp.dma_start(small_ids_sb[:], small_ids.partition_broadcast(P)).then_inc(small_ids_loaded, 16)
            sp.dma_start(small_iota_sb[:], small_iota).then_inc(small_ids_loaded, 16)
            for x in range(ONE_HOT):
                table = tables[ONE_HOT_FEATURES[x]].rearrange("(p k) d -> p k d", k=SMALL_K)
                for a, b in ((0, SPRAY), (SPRAY, SMALL_P)):
                    sp.dma_start(small[x][a:b, :, :], table[a:b, :, :]).then_inc(small_loaded[x], 16)
            for k in range(SLOTS):
                sp.dma_start(rows[k][:, entry(BOTTOM), :], bottom[k * P:(k + 1) * P, :]).then_inc(bottom_loaded[k], 16)
            sp.dma_start(wp[:], w_pairs).then_inc(weights_loaded, 16)
            sp.dma_start(wb[:], w_bottom).then_inc(weights_loaded, 16)
            sp.dma_start(w2_sb[:], w2.rearrange("(k p) n -> p k n", p=P)).then_inc(weights_loaded, 16)
            sp.dma_start(b1_sb[:], b1).then_inc(weights_loaded, 16)
            sp.dma_start(b2_sb[:], b2).then_inc(weights_loaded, 16)
            sp.dma_start(w3_sb[:], w3).then_inc(weights_loaded, 16)
            with sp.Fori(0, PAIRS_OF_TILES - 1) as i:
                for k in range(SLOTS):
                    sp.wait_ge(rows_transposed, (i * SLOTS + k + 1) * NC)
                    sp.dma_start(rows[k][:, entry(BOTTOM), :],
                                 bottom[bass.ds((i + 1) * (SLOTS * P) + k * P, P), :]).then_inc(bottom_loaded[k], 16)
            sp.wait_ge(y_written, 1 + TILES)
            sp.dma_start(out, y_sb[:]).then_inc(y_stored, 16)
            sp.wait_ge(y_stored, 16)

        @block.gpsimd
        def _(pool):
            nc.gpsimd.memset(ident[:], 0.0).then_inc(ident_zeroed, 1)
            pool.wait_ge(ident_zeroed, 1)
            nc.gpsimd.affine_select(out=ident[:], in_=ident[:], compare_op=ALU.not_equal, fill=1.0, base=0,
                                    pattern=[[-1, P]], channel_multiplier=1).then_inc(ident_ready, 1)
            pool.wait_ge(ids_loaded, 16)
            for t in range(TILES):
                i, k = divmod(t, SLOTS)
                if i:
                    pool.wait_ge(rows_transposed, (t - SLOTS + 1) * NC)
                for c, chunk in enumerate(CHUNKS):
                    for e in chunk:
                        if ONE_HOT <= e < BOTTOM:
                            at = t * FEATURES + ORDER[e]
                            nc.gpsimd.indirect_dma_start(
                                out=rows[k][:, entry(e), :], out_offset=None, in_=tables[ORDER[e]],
                                in_offset=bass.IndirectOffsetOnAxis(ap=ids_sb[:, at:at + 1], axis=0),
                            ).then_inc(gathered[k][c], 16)

        @block.tensor
        def _(pe):
            pe.wait_ge(ident_ready, 1)
            pe.wait_ge(one_hot_ready, ONE_HOT)
            for x in range(ONE_HOT):
                pe.wait_ge(small_loaded[x], 32)

            with pe.Fori(0, PAIRS_OF_TILES) as i:
                def rows_to_columns(k):
                    for c, entries in enumerate(CHUNKS):
                        bank = ps_rows[(k * NC + c) % BANKS]
                        gathers = sum(ONE_HOT <= e < BOTTOM for e in entries)
                        if gathers:
                            pe.wait_ge(gathered[k][c], (i + 1) * (16 * gathers))
                        if BOTTOM in entries:
                            pe.wait_ge(bottom_loaded[k], (i + 1) * 16)
                        pe.wait_ge(rowsT_written, (i * SLOTS + k) * NC + c + 1)
                        for j, e in enumerate(entries):
                            if e < ONE_HOT:
                                for r in range(SMALL_K):
                                    last = nc.tensor.matmul(
                                        bank[:, j, :], small[e][0:SMALL_P, r, :],
                                        one_hot[0:SMALL_P, e * SMALL_K + r, bass.ds((i * SLOTS + k) * P, P)],
                                        start=r == 0, stop=r == SMALL_K - 1)
                            else:
                                last = nc.tensor.transpose(bank[:, j, :], rows[k][:, entry(e), :], ident[:])
                        last.then_inc(rows_transposed, 1)

                def products(k):
                    pe.wait_ge(rowsT_written, (i * SLOTS + k) * NC + (NC + BANKS))
                    for b in range(NB):
                        pe.wait_ge(taken_act, (i * SLOTS + k) * NB + b + 1)
                        pe.wait_ge(taken_dve, (i * SLOTS + k) * NB + b + 1)
                        for m in range(PPB):
                            s0 = (b * PPB + m) * PACK
                            at = m * PACK * COLUMNS
                            last = nc.tensor.matmul(
                                ps_prod[b % BANKS][:, at:at + PACK * COLUMNS].rearrange("p (s g) -> p s g", s=PACK),
                                rowsT[k][:, s0:s0 + PACK, :].rearrange("p s f -> p (s f)"),
                                rowsT[k][:, s0:s0 + PACK, 1:FEATURES], start=True, stop=True)
                        last.then_inc(products_done, 1)

                def layer1(k):
                    if k == 0:
                        pe.wait_ge(weights_loaded, 16 * WEIGHT_LOADS)
                        pe.wait_ge(wb_summed, 1)
                    pe.wait_ge(y_written, i * SLOTS + k + 1)
                    for n in range(N1):
                        nc.tensor.matmul(ps_acc[n][:, 0:P], wb_sum[:, n * P:(n + 1) * P], bottomT[k][:],
                                         start=True, stop=False)
                    pe.wait_ge(taken_act, (i * SLOTS + k) * NB + (NB + BANKS))
                    pe.wait_ge(taken_dve, (i * SLOTS + k) * NB + (NB + BANKS))
                    for n in range(N1):
                        for g in range(GROUPS):
                            last = nc.tensor.matmul(ps_acc[n][:, 0:P], wp[:, g, n * P:(n + 1) * P], pairs[k][:, g, :],
                                                    start=False, stop=g == GROUPS - 1)
                        last.then_inc(layer1_done, 1)

                def layers_2_and_3(k):
                    for blocks in (range(N1 - 1), range(N1 - 1, N1)):
                        pe.wait_ge(h1_written, (i * SLOTS + k) * N1 + blocks[-1] + 1)
                        for m in range(N2):
                            for n in blocks:
                                last = nc.tensor.matmul(ps_acc[m][:, 0:P], w2_sb[:, n, m * P:(m + 1) * P], h1[:, n, :],
                                                        start=n == 0, stop=n == N1 - 1)
                            if blocks[-1] == N1 - 1:
                                last.then_inc(layer2_done, 1)
                            elif m == 0:
                                last.then_inc(slot_free[k], 1)
                    for m in range(N2):
                        pe.wait_ge(h2_written, (i * SLOTS + k) * N2 + m + 1)
                        last = nc.tensor.matmul(ps_acc[Y_BANK][0:1, 0:P], w3_sb[:, m:m + 1], h2[:, m, :],
                                                start=m == 0, stop=m == N2 - 1)
                    last.then_inc(layer3_done, 1)

                rows_to_columns(0)
                products(0)
                layer1(0)
                rows_to_columns(1)
                layers_2_and_3(0)
                products(1)
                layer1(1)
                layers_2_and_3(1)

        @block.vector
        def _(dve):
            dve.wait_ge(small_ids_loaded, 32)
            for x in range(ONE_HOT):
                for r in range(SMALL_K):
                    last = nc.vector.tensor_scalar(one_hot[:, x * SMALL_K + r, :], small_ids_sb[:, x, :],
                                                   small_iota_sb[:, r:r + 1], None, ALU.is_equal)
                last.then_inc(one_hot_ready, 1)
            for k in range(SLOTS):
                nc.vector.memset(pairs[k][FILLED:P, GROUPS - 1, :], 0.0)
                nc.vector.memset(rowsT[k][:, :, FEATURES:QUADRANT], 0.0).then_inc(slot_free[k], 1)
            for b in range(BANKS):
                dve.sem_inc(rowsT_written, 1)
                dve.sem_inc(taken_dve, 1)
                dve.sem_inc(taken_act, 1)
            dve.sem_inc(y_written, 1)
            dve.wait_ge(weights_loaded, 16 * WEIGHT_LOADS)
            nc.vector.tensor_tensor(wb_sum[:], wb[:, 0, :], wb[:, 1, :], ALU.add).then_inc(wb_summed, 1)

            with dve.Fori(0, PAIRS_OF_TILES) as i:
                for k in range(SLOTS):
                    dve.wait_ge(slot_free[k], i + 1)
                    for c, entries in enumerate(CHUNKS):
                        dve.wait_ge(rows_transposed, (i * SLOTS + k) * NC + c + 1)
                        bank = ps_rows[(k * NC + c) % BANKS]
                        j = 0
                        if entries[0] == BOTTOM:
                            nc.vector.tensor_copy(bottomT[k][:], bank[:, 0, :])
                            j = 1
                        nc.vector.tensor_copy(
                            rowsT[k][:, :, entries[j]:entries[-1] + 1].rearrange("p s f -> p f s"),
                            bank[:, j:len(entries), :]).then_inc(rowsT_written, 1)
                    for b in range(NB):
                        dve.wait_ge(products_done, (i * SLOTS + k) * NB + b + 1)
                        take_products(nc.vector.tensor_copy, k, b, range(PACK // 2, PACK)).then_inc(taken_dve, 1)

        @block.scalar
        def _(act):
            act.wait_ge(weights_loaded, 16 * WEIGHT_LOADS)
            with act.Fori(0, PAIRS_OF_TILES) as i:
                for k in range(SLOTS):
                    act.wait_ge(slot_free[k], i + 1)
                    for b in range(NB):
                        act.wait_ge(products_done, (i * SLOTS + k) * NB + b + 1)
                        take_products(nc.scalar.copy, k, b, range(PACK // 2)).then_inc(taken_act, 1)
                    for n in range(N1):
                        act.wait_ge(layer1_done, (i * SLOTS + k) * N1 + n + 1)
                        nc.scalar.activation(h1[:, n, :], ps_acc[n][:, 0:P], ACT.Relu,
                                             bias=b1_sb[:, n:n + 1]).then_inc(h1_written, 1)
                    for m in range(N2):
                        act.wait_ge(layer2_done, (i * SLOTS + k) * N2 + m + 1)
                        nc.scalar.activation(h2[:, m, :], ps_acc[m][:, 0:P], ACT.Relu,
                                             bias=b2_sb[:, m:m + 1]).then_inc(h2_written, 1)
                    act.wait_ge(layer3_done, i * SLOTS + k + 1)
                    nc.scalar.copy(y_sb[0:1, bass.ds((i * SLOTS + k) * P, P)],
                                   ps_acc[Y_BANK][0:1, 0:P]).then_inc(y_written, 1)


def kernel(**inputs):
    import numpy as np
    import concourse.bacc as bacc
    from concourse.bass_utils import run_bass_kernel_spmd

    w1 = np.asarray(inputs["W_top1"])
    w_pairs = np.zeros((P, GROUPS, HIDDEN1), w1.dtype)
    for g in range(1, FEATURES):
        for a in range(g):
            lo, hi = sorted((ORDER[a], ORDER[g]))
            group, q = divmod(g - 1, PACK)
            w_pairs[q * QUADRANT + a, group] = w1[DIM + hi * (hi - 1) // 2 + lo]
    ids = np.ascontiguousarray(inputs["ids"]).view(np.uint32)
    arrays = {
        "bottom": inputs["r_bottom_mlp_out"],
        "ids": ids,
        "small_ids": ids[:, ONE_HOT_FEATURES].T,
        "small_iota": np.arange(P * SMALL_K, dtype=np.float32).reshape(P, SMALL_K),
        **{f"tbl_{f}": inputs[f"tbl_{f}"] for f in range(FEATURES)},
        "w_pairs": w_pairs,
        "w_bottom": np.stack([w1[:DIM], w1[-DIM:]], axis=1),
        "b1": np.asarray(inputs["b_top1"]).reshape(N1, P).T,
        "w2": inputs["W_top2"],
        "b2": np.asarray(inputs["b_top2"]).reshape(N2, P).T,
        "w3": np.asarray(inputs["W_top3"]).reshape(N2, P).T,
    }
    arrays = {name: np.ascontiguousarray(a) for name, a in arrays.items()}

    nc = bacc.Bacc("TRN2", target_bir_lowering=False, num_devices=1)
    aps = {name: nc.dram_tensor(name, a.shape, mybir.dt.from_np(a.dtype), kind="ExternalInput").ap()
           for name, a in arrays.items()}
    out = nc.dram_tensor("out", (1, BATCH), mybir.dt.float32, kind="ExternalOutput").ap()
    dlrm_tower(nc, aps["bottom"], aps["ids"], aps["small_ids"], aps["small_iota"],
               [aps[f"tbl_{f}"] for f in range(FEATURES)], aps["w_pairs"], aps["w_bottom"],
               aps["b1"], aps["w2"], aps["b2"], aps["w3"], out)
    r = run_bass_kernel_spmd(nc, [arrays], core_ids=[0])
    return r.results[0]["out"].reshape(BATCH, 1)
```

```python
import concourse.bass as bass
from concourse import mybir
from contextlib import ExitStack

BATCH, FEATURES, DIM = 512, 27, 128
HIDDEN1, HIDDEN2 = 512, 256
TABLE_ROWS = [1250, 1000, 125000, 1250, 1000, 1000, 12500, 12500, 1000, 1250, 12500, 12500, 12500, 1250,
              12500, 12500, 1000, 12500, 1000, 1000, 1000, 1250, 1000, 1250, 1000, 1000, 1250]
P = 128
TILES = BATCH // P
SLOTS = 2
PAIRS_OF_TILES = TILES // SLOTS

ONE_HOT = 5
SMALL_ROWS = 1000
SMALL_P = 125
SMALL_K = SMALL_ROWS // SMALL_P
SPRAY = SMALL_P // 16 * 16
RAW = 3
SPLITS = 2
PARTS = 3
ONE_HOT_FEATURES = [f for f in range(FEATURES) if TABLE_ROWS[f] == SMALL_ROWS][:ONE_HOT]

ORDER = ONE_HOT_FEATURES + [f for f in range(FEATURES) if f not in ONE_HOT_FEATURES]
FPC = 4
CHUNKS = [list(range(a, min(a + FPC, FEATURES))) for a in range(ONE_HOT, FEATURES, FPC)]
NC = len(CHUNKS)

QUADRANT = 32
PACK = P // QUADRANT
COLUMNS = FEATURES - 1
GROUPS = -(-COLUMNS // PACK)
PPB = 4
NB = P // (PACK * PPB)
ROWS_USED = FEATURES - 1
ACROSS = (PACK - 1) * QUADRANT + ROWS_USED
BANKS = 5
FIRST_BANK = NB % BANKS
COPIERS = 2
BEFORE_LAYER1 = NC // 2
N1 = HIDDEN1 // P
N2 = HIDDEN2 // P
NPB = N1 // 2

FILLED = COLUMNS % PACK * QUADRANT
STRIP = QUADRANT - FEATURES + 1
B_GROUP = 3
B_GROUPS = GROUPS - B_GROUP
STRIPS = [(q * QUADRANT + FEATURES - 1, GROUPS if q == 0 else GROUPS - 1) for q in range(PACK)]
B_PLACES = ([(p, GROUPS - 1) for p in range(FILLED, P)]
            + [(start + r, g) for start, end in STRIPS for r in range(STRIP) for g in range(B_GROUP, end)])
B_LOADS = 1 + len(STRIPS)
assert len(B_PLACES) >= DIM and FILLED == 2 * QUADRANT


def bank_of_chunk(c):
    return (FIRST_BANK + c) % BANKS


def last_product_before(c):
    return max(b for b in range(NB) if b % BANKS == bank_of_chunk(c))


def dlrm_tower(nc, bottom, ids, small_ids, small_iota, tables, w_first, w_last, b1, w2, b2, w3, out):
    fp32 = mybir.dt.float32
    bf16 = mybir.dt.bfloat16
    fp16 = mybir.dt.float16
    u32 = mybir.dt.uint32
    ALU = mybir.AluOpType
    ACT = mybir.ActivationFunctionType

    with ExitStack() as ctx:
        def sb(name, shape, dt=fp32):
            return ctx.enter_context(nc.sbuf_tensor(name, shape, dt))

        def ps(name, shape):
            return ctx.enter_context(nc.psum_tensor(name, shape, fp32))

        def sem(name):
            return ctx.enter_context(nc.semaphore(name))

        ids_sb = sb("ids_sb", [P, TILES * FEATURES], u32)
        small_ids_sb = sb("small_ids_sb", [P, ONE_HOT, BATCH], u32)
        small_ids16 = sb("small_ids16", [P, ONE_HOT, BATCH], fp16)
        small_iota_sb = sb("small_iota_sb", [P, SMALL_K])
        raw = [sb(f"raw{h}", [P, SMALL_K, DIM]) for h in range(RAW)]
        rest = sb("rest", [P, SMALL_K, DIM])
        part = [[sb(f"part{h}_{j}", [P, SMALL_K, DIM], bf16) for j in range(PARTS)] for h in range(SPLITS)]
        one_hot = [sb(f"one_hot{h}", [P, SMALL_K, BATCH], bf16) for h in range(SPLITS)]
        selected = sb("selected", [DIM, ONE_HOT, BATCH])
        rows = [sb(f"rows{k}", [P, FEATURES - ONE_HOT, DIM]) for k in range(SLOTS)]
        rowsT = [sb(f"rowsT{k}", [DIM, P, QUADRANT]) for k in range(SLOTS)]
        pairs = [sb(f"pairs{k}", [P, GROUPS, P]) for k in range(SLOTS)]
        ident = sb("ident", [P, P])
        wp = sb("wp", [P, GROUPS, HIDDEN1])
        wl = sb("wl", [P, B_GROUPS, HIDDEN1])
        w2_sb = sb("w2_sb", [P, N1, HIDDEN2])
        w3_sb = sb("w3_sb", [P, N2])
        b1_sb = sb("b1_sb", [P, N1])
        b2_sb = sb("b2_sb", [P, N2])
        h1 = sb("h1", [P, N1, P])
        h2 = sb("h2", [P, N2, P])
        y_sb = sb("y_sb", [1, BATCH])

        ps_work = [ps(f"ps_work{i}", [P, BATCH]) for i in range(BANKS)]
        ps_acc = [ps(f"ps_acc{i}", [P, BATCH]) for i in range(3)]
        ACC = len(ps_acc)
        L2_BANK = [0, 2]
        L3_BANK = 1

        ids_loaded = sem("ids_loaded")
        small_iota_loaded = sem("small_iota_loaded")
        small_ids_loaded = [sem(f"small_ids_loaded{h}") for h in range(2)]
        raw_loaded = [sem(f"raw_loaded{h}") for h in range(RAW)]
        weights_loaded = sem("weights_loaded")
        ident_zeroed = sem("ident_zeroed")
        ident_ready = sem("ident_ready")
        weights_summed = sem("weights_summed")
        ids16_ready = sem("ids16_ready")
        one_hot_ready = sem("one_hot_ready")
        part_ready = [sem(f"part_ready{j}") for j in range(PARTS)]
        rest_ready = sem("rest_ready")
        one_hot_used = sem("one_hot_used")
        selected_ready = sem("selected_ready")
        selected_placed = sem("selected_placed")
        gathered = [[sem(f"gathered{k}_{c}") for c in range(NC)] for k in range(SLOTS)]
        bottom_loaded = [sem(f"bottom_loaded{k}") for k in range(SLOTS)]
        rows_transposed = sem("rows_transposed")
        placed = [sem("placed_dve"), sem("placed_act")]
        products_done = sem("products_done")
        taken = [sem("taken_dve"), sem("taken_act")]
        slot_free = [sem(f"slot_free{k}") for k in range(SLOTS)]
        layer1_done = sem("layer1_done")
        layer2_done = sem("layer2_done")
        layer3_done = sem("layer3_done")
        h1_written = sem("h1_written")
        h2_written = sem("h2_written")
        y_written = sem("y_written")
        y_stored = sem("y_stored")

        WEIGHT_LOADS = 6

        PLACED = [len(range(e, NC, COPIERS)) for e in range(COPIERS)]

        def load_small(queue, x):
            table = tables[ONE_HOT_FEATURES[x]].rearrange("(p k) d -> p k d", k=SMALL_K)
            for a, b in ((0, SPRAY), (SPRAY, SMALL_P)):
                queue.dma_start(raw[x % RAW][a:b, :, :], table[a:b, :, :]).then_inc(raw_loaded[x % RAW], 16)

        def load_bottom(sp, k, samples):
            spots = [(slice(FILLED, P), GROUPS - 1, GROUPS)] + [
                (slice(start, start + STRIP), B_GROUP, end) for start, end in STRIPS]
            for partitions, g0, g1 in spots:
                sp.dma_start(pairs[k][partitions, g0:g1, :],
                             bottom[partitions, g0 - B_GROUP:g1 - B_GROUP, samples]).then_inc(bottom_loaded[k], 16)

        def place_rows(engine_copy, k, c):
            entries = CHUNKS[c]
            return engine_copy(rowsT[k][:, :, entries[0]:entries[-1] + 1].rearrange("p s f -> p f s"),
                               ps_work[bank_of_chunk(c)][:, 0:len(entries) * P].rearrange("p (f s) -> p f s", s=P))

        def take_products(engine_copy, k, b, samples):
            src = ps_work[b % BANKS][:, 0:PPB * PACK * COLUMNS].rearrange("p (m s g) -> p m s g", m=PPB, s=PACK)
            first = b * PPB * PACK
            dst = pairs[k][:, :, first:first + PPB * PACK].rearrange("p g (m s) -> p m s g", s=PACK)
            last = None
            for s in samples:
                for q in range(PACK):
                    n = -(-(COLUMNS - q) // PACK)
                    last = engine_copy(
                        dst[q * QUADRANT:q * QUADRANT + ROWS_USED, :, s, 0:n],
                        src[s * QUADRANT:s * QUADRANT + ROWS_USED, :, s, q:q + (n - 1) * PACK + 1:PACK])
            return last

        block = ctx.enter_context(nc.Block())

        @block.sync
        def _(sp):
            sp.dma_start(ids_sb[:].rearrange("p (t f) -> p t f", f=FEATURES),
                         ids.rearrange("(t p) f -> p t f", p=P)).then_inc(ids_loaded, 16)
            sp.dma_start(small_ids_sb[:, 0:1, :], small_ids[0:1, :].partition_broadcast(P)).then_inc(small_ids_loaded[0], 16)
            sp.dma_start(small_iota_sb[:], small_iota).then_inc(small_iota_loaded, 16)
            sp.dma_start(small_ids_sb[:, 1:ONE_HOT, :], small_ids[1:ONE_HOT, :].partition_broadcast(P)
                         ).then_inc(small_ids_loaded[1], 16)
            for x in range(1, RAW):
                load_small(sp, x)
            sp.dma_start(wp[:], w_first).then_inc(weights_loaded, 16)
            sp.dma_start(wl[:], w_last).then_inc(weights_loaded, 16)
            sp.dma_start(w2_sb[:], w2.rearrange("(k p) n -> p k n", p=P)).then_inc(weights_loaded, 16)
            sp.dma_start(b1_sb[:], b1).then_inc(weights_loaded, 16)
            sp.dma_start(b2_sb[:], b2).then_inc(weights_loaded, 16)
            sp.dma_start(w3_sb[:], w3).then_inc(weights_loaded, 16)
            for x in range(RAW, ONE_HOT):
                sp.wait_ge(rest_ready, x - RAW + 1)
                load_small(sp, x)
            for k in range(SLOTS):
                load_bottom(sp, k, slice(k * P, (k + 1) * P))
            with sp.Fori(0, PAIRS_OF_TILES - 1) as i:
                for k in range(SLOTS):
                    sp.wait_ge(slot_free[k], i + 2)
                    load_bottom(sp, k, bass.ds((i + 1) * (SLOTS * P) + k * P, P))
            sp.wait_ge(y_written, 1 + TILES)
            sp.dma_start(out, y_sb[:]).then_inc(y_stored, 16)
            sp.wait_ge(y_stored, 16)

        @block.gpsimd
        def _(pool):
            nc.gpsimd.memset(ident[:], 0.0).then_inc(ident_zeroed, 1)
            pool.wait_ge(ident_zeroed, 1)
            nc.gpsimd.affine_select(out=ident[:], in_=ident[:], compare_op=ALU.not_equal, fill=1.0, base=0,
                                    pattern=[[-1, P]], channel_multiplier=1).then_inc(ident_ready, 1)
            pool.wait_ge(ids_loaded, 16)
            for t in range(TILES):
                i, k = divmod(t, SLOTS)
                if i:
                    pool.wait_ge(rows_transposed, (t - SLOTS + 1) * NC)
                for c, entries in enumerate(CHUNKS):
                    for e in entries:
                        at = t * FEATURES + ORDER[e]
                        nc.gpsimd.indirect_dma_start(
                            out=rows[k][:, e - ONE_HOT, :], out_offset=None, in_=tables[ORDER[e]],
                            in_offset=bass.IndirectOffsetOnAxis(ap=ids_sb[:, at:at + 1], axis=0),
                        ).then_inc(gathered[k][c], 16)

        @block.tensor
        def _(pe):
            for x in range(ONE_HOT):
                if x >= ACC:
                    pe.wait_ge(selected_ready, x - ACC + 1)
                for j in range(PARTS):
                    pe.wait_ge(part_ready[j], x + 1)
                    for r in range(SMALL_K):
                        if j == 0:
                            pe.wait_ge(one_hot_ready, x * SMALL_K + r + 1)
                        last = nc.tensor.matmul(
                            ps_acc[x % ACC][:], part[x % SPLITS][j][0:SMALL_P, r, :],
                            one_hot[x % SPLITS][0:SMALL_P, r, :],
                            start=j == 0 and r == 0, stop=j == PARTS - 1 and r == SMALL_K - 1)
                last.then_inc(one_hot_used, 1)
            pe.wait_ge(selected_ready, ONE_HOT)
            pe.wait_ge(ident_ready, 1)

            with pe.Fori(0, PAIRS_OF_TILES) as i:
                def transposes(k, chunks):
                    for c in chunks:
                        pe.wait_ge(gathered[k][c], (i + 1) * (16 * len(CHUNKS[c])))
                        if c >= BANKS:
                            e = (c - BANKS) % COPIERS
                            pe.wait_ge(placed[e], (i * SLOTS + k) * PLACED[e] + (c - BANKS) // COPIERS + 1)
                        else:
                            for e in taken:
                                pe.wait_ge(e, (i * SLOTS + k) * NB + last_product_before(c) + 1)
                        for j, position in enumerate(CHUNKS[c]):
                            last = nc.tensor.transpose(ps_work[bank_of_chunk(c)][:, j * P:(j + 1) * P],
                                                       rows[k][:, position - ONE_HOT, :], ident[:])
                        last.then_inc(rows_transposed, 1)

                def products(k):
                    pe.wait_ge(selected_placed, i * SLOTS + k + 1)
                    for e in range(COPIERS):
                        pe.wait_ge(placed[e], (i * SLOTS + k + 1) * PLACED[e])
                    for b in range(NB):
                        if b >= BANKS:
                            for e in taken:
                                pe.wait_ge(e, (i * SLOTS + k + 1) * NB + b - BANKS + 1)
                        for m in range(PPB):
                            s0 = (b * PPB + m) * PACK
                            at = m * PACK * COLUMNS
                            last = nc.tensor.matmul(
                                ps_work[b % BANKS][0:ACROSS, at:at + PACK * COLUMNS].rearrange(
                                    "p (s g) -> p s g", s=PACK),
                                rowsT[k][:, s0:s0 + PACK, :].rearrange("p s f -> p (s f)")[:, 0:ACROSS],
                                rowsT[k][:, s0:s0 + PACK, 1:FEATURES], start=True, stop=True)
                        last.then_inc(products_done, 1)

                def layer1(k):
                    if k == 0:
                        pe.wait_ge(weights_loaded, 16 * WEIGHT_LOADS)
                        pe.wait_ge(weights_summed, 1)
                    pe.wait_ge(y_written, i * SLOTS + k + 1)
                    pe.wait_ge(bottom_loaded[k], (i + 1) * (16 * B_LOADS))
                    for e in taken:
                        pe.wait_ge(e, (i * SLOTS + k + 2) * NB)
                    for n in range(N1):
                        for g in range(GROUPS):
                            last = nc.tensor.matmul(ps_acc[n // NPB][:, (n % NPB) * P:(n % NPB + 1) * P],
                                                    wp[:, g, n * P:(n + 1) * P], pairs[k][:, g, :],
                                                    start=g == 0, stop=g == GROUPS - 1)
                        if n % NPB == NPB - 1:
                            last.then_inc(layer1_done, 1)

                def layers_2_and_3(k):
                    for blocks in (range(NPB), range(NPB, N1)):
                        pe.wait_ge(h1_written, (i * SLOTS + k) * N1 + blocks[-1] + 1)
                        for m in range(N2):
                            for n in blocks:
                                last = nc.tensor.matmul(ps_acc[L2_BANK[m]][:, 0:P], w2_sb[:, n, m * P:(m + 1) * P],
                                                        h1[:, n, :], start=n == 0, stop=n == N1 - 1)
                            if blocks[-1] == N1 - 1:
                                last.then_inc(layer2_done, 1)
                            elif m == 0:
                                last.then_inc(slot_free[k], 1)
                    for m in range(N2):
                        pe.wait_ge(h2_written, (i * SLOTS + k) * N2 + m + 1)
                        last = nc.tensor.matmul(ps_acc[L3_BANK][0:1, 0:P], w3_sb[:, m:m + 1], h2[:, m, :],
                                                start=m == 0, stop=m == N2 - 1)
                    last.then_inc(layer3_done, 1)

                transposes(0, range(NC))
                products(0)
                transposes(1, range(BEFORE_LAYER1))
                layer1(0)
                transposes(1, range(BEFORE_LAYER1, NC))
                layers_2_and_3(0)
                products(1)
                layer1(1)
                layers_2_and_3(1)

        @block.vector
        def _(dve):
            for k in range(SLOTS):
                nc.vector.memset(pairs[k][:, 0:B_GROUP, :], 0.0)
                nc.vector.memset(pairs[k][QUADRANT:FILLED, GROUPS - 1, :], 0.0)
                nc.vector.memset(rowsT[k][:, :, FEATURES:QUADRANT], 0.0).then_inc(slot_free[k], 1)
            for s in taken:
                dve.sem_inc(s, NB)
            dve.sem_inc(y_written, 1)
            dve.wait_ge(small_iota_loaded, 16)
            for x in range(ONE_HOT):
                dve.wait_ge(small_ids_loaded[min(x, 1)], 16)
                nc.vector.tensor_copy(small_ids16[:, x, :], small_ids_sb[:, x, :]).then_inc(ids16_ready, 1)
                if x >= SPLITS:
                    dve.wait_ge(one_hot_used, x - SPLITS + 1)

                def one_hots():
                    dve.wait_ge(ids16_ready, x + 1)
                    for r in range(SMALL_K):
                        nc.vector.tensor_scalar(one_hot[x % SPLITS][:, r, :], small_ids16[:, x, :],
                                                small_iota_sb[:, r:r + 1], None, ALU.is_equal).then_inc(one_hot_ready, 1)

                if x == 0:
                    one_hots()
                dve.wait_ge(raw_loaded[x % RAW], 32 * (x // RAW + 1))
                dve.wait_ge(part_ready[0], x + 1)
                if x >= 1:
                    dve.wait_ge(part_ready[2], x)
                nc.vector.tensor_tensor(rest[0:SMALL_P], raw[x % RAW][0:SMALL_P], part[x % SPLITS][0][0:SMALL_P],
                                        ALU.subtract).then_inc(rest_ready, 1)
                if x > 0:
                    one_hots()
                dve.wait_ge(part_ready[1], x + 1)
                nc.vector.tensor_tensor(part[x % SPLITS][2][0:SMALL_P], rest[0:SMALL_P], part[x % SPLITS][1][0:SMALL_P],
                                        ALU.subtract).then_inc(part_ready[2], 1)
            dve.wait_ge(weights_loaded, 16 * WEIGHT_LOADS)
            nc.vector.tensor_tensor(wp[:, B_GROUP:GROUPS, :], wp[:, B_GROUP:GROUPS, :], wl[:],
                                    ALU.add).then_inc(weights_summed, 1)

            with dve.Fori(0, PAIRS_OF_TILES) as i:
                for k in range(SLOTS):
                    dve.wait_ge(slot_free[k], i + 1)
                    for c in range(0, NC, COPIERS):
                        dve.wait_ge(rows_transposed, (i * SLOTS + k) * NC + c + 1)
                        place_rows(nc.vector.tensor_copy, k, c).then_inc(placed[0], 1)
                    for b in range(NB):
                        dve.wait_ge(products_done, (i * SLOTS + k) * NB + b + 1)
                        take_products(nc.vector.tensor_copy, k, b, range(PACK // 2, PACK)).then_inc(taken[0], 1)

        @block.scalar
        def _(act):
            def first_part(x):
                act.wait_ge(raw_loaded[x % RAW], 32 * (x // RAW + 1))
                if x >= SPLITS:
                    act.wait_ge(one_hot_used, x - SPLITS + 1)
                nc.scalar.copy(part[x % SPLITS][0][0:SMALL_P], raw[x % RAW][0:SMALL_P]).then_inc(part_ready[0], 1)

            def copy_selected(x):
                act.wait_ge(one_hot_used, x + 1)
                nc.scalar.copy(selected[:, x, :], ps_acc[x % ACC][:]).then_inc(selected_ready, 1)

            load_small(act, 0)
            first_part(0)
            for x in range(ONE_HOT):
                act.wait_ge(rest_ready, x + 1)
                nc.scalar.copy(part[x % SPLITS][1][0:SMALL_P], rest[0:SMALL_P]).then_inc(part_ready[1], 1)
                if x >= 1:
                    copy_selected(x - 1)
                if x + 1 < ONE_HOT:
                    first_part(x + 1)
            copy_selected(ONE_HOT - 1)
            act.wait_ge(selected_ready, ONE_HOT)
            act.wait_ge(weights_loaded, 16 * WEIGHT_LOADS)

            with act.Fori(0, PAIRS_OF_TILES) as i:
                def place(k, chunks):
                    if 0 in chunks:
                        act.wait_ge(slot_free[k], i + 1)
                        nc.scalar.copy(rowsT[k][:, :, 0:ONE_HOT].rearrange("p s f -> p f s"),
                                       selected[:, :, bass.ds((i * SLOTS + k) * P, P)]).then_inc(selected_placed, 1)
                    for c in (c for c in chunks if c % COPIERS == 1):
                        act.wait_ge(rows_transposed, (i * SLOTS + k) * NC + c + 1)
                        place_rows(nc.scalar.copy, k, c).then_inc(placed[1], 1)

                def take(k):
                    for b in range(NB):
                        act.wait_ge(products_done, (i * SLOTS + k) * NB + b + 1)
                        take_products(nc.scalar.copy, k, b, range(PACK // 2)).then_inc(taken[1], 1)

                def take_layer1(k):
                    for n in range(N1):
                        if n % NPB == 0:
                            act.wait_ge(layer1_done, (i * SLOTS + k) * 2 + n // NPB + 1)
                        nc.scalar.activation(h1[:, n, :], ps_acc[n // NPB][:, (n % NPB) * P:(n % NPB + 1) * P],
                                             ACT.Relu, bias=b1_sb[:, n:n + 1]).then_inc(h1_written, 1)

                def take_layers_2_and_3(k):
                    for m in range(N2):
                        act.wait_ge(layer2_done, (i * SLOTS + k) * N2 + m + 1)
                        nc.scalar.activation(h2[:, m, :], ps_acc[L2_BANK[m]][:, 0:P], ACT.Relu,
                                             bias=b2_sb[:, m:m + 1]).then_inc(h2_written, 1)
                    act.wait_ge(layer3_done, i * SLOTS + k + 1)
                    nc.scalar.copy(y_sb[0:1, bass.ds((i * SLOTS + k) * P, P)],
                                   ps_acc[L3_BANK][0:1, 0:P]).then_inc(y_written, 1)

                place(0, range(NC))
                take(0)
                place(1, range(BEFORE_LAYER1))
                take_layer1(0)
                place(1, range(BEFORE_LAYER1, NC))
                take_layers_2_and_3(0)
                take(1)
                take_layer1(1)
                take_layers_2_and_3(1)


def kernel(**inputs):
    import numpy as np
    import concourse.bacc as bacc
    from concourse.bass_utils import run_bass_kernel_spmd

    w1 = np.asarray(inputs["W_top1"])
    w_first = np.zeros((P, GROUPS, HIDDEN1), w1.dtype)
    w_last = np.zeros((P, B_GROUPS, HIDDEN1), w1.dtype)
    for g in range(1, FEATURES):
        for a in range(g):
            lo, hi = sorted((ORDER[a], ORDER[g]))
            group, q = divmod(g - 1, PACK)
            w_first[q * QUADRANT + a, group] = w1[DIM + hi * (hi - 1) // 2 + lo]
    bottom = np.zeros((P, B_GROUPS, BATCH), np.float32)
    for d, (p, g) in zip(range(DIM), B_PLACES):
        w_first[p, g] = w1[d]
        w_last[p, g - B_GROUP] = w1[d - DIM]
        bottom[p, g - B_GROUP] = np.asarray(inputs["r_bottom_mlp_out"])[:, d]
    ids = np.ascontiguousarray(inputs["ids"]).view(np.uint32)
    arrays = {
        "bottom": bottom,
        "ids": ids,
        "small_ids": ids[:, ONE_HOT_FEATURES].T,
        "small_iota": np.arange(P * SMALL_K, dtype=np.float32).reshape(P, SMALL_K),
        **{f"tbl_{f}": inputs[f"tbl_{f}"] for f in range(FEATURES)},
        "w_first": w_first,
        "w_last": w_last,
        "b1": np.asarray(inputs["b_top1"]).reshape(N1, P).T,
        "w2": inputs["W_top2"],
        "b2": np.asarray(inputs["b_top2"]).reshape(N2, P).T,
        "w3": np.asarray(inputs["W_top3"]).reshape(N2, P).T,
    }
    arrays = {name: np.ascontiguousarray(a) for name, a in arrays.items()}

    nc = bacc.Bacc("TRN2", target_bir_lowering=False, num_devices=1)
    aps = {name: nc.dram_tensor(name, a.shape, mybir.dt.from_np(a.dtype), kind="ExternalInput").ap()
           for name, a in arrays.items()}
    out = nc.dram_tensor("out", (1, BATCH), mybir.dt.float32, kind="ExternalOutput").ap()
    dlrm_tower(nc, aps["bottom"], aps["ids"], aps["small_ids"], aps["small_iota"],
               [aps[f"tbl_{f}"] for f in range(FEATURES)], aps["w_first"], aps["w_last"],
               aps["b1"], aps["w2"], aps["b2"], aps["w3"], out)
    r = run_bass_kernel_spmd(nc, [arrays], core_ids=[0])
    return r.results[0]["out"].reshape(BATCH, 1)
```

```python
import concourse.bass as bass
from concourse import mybir
from contextlib import ExitStack

BATCH, FEATURES, DIM = 512, 27, 128
HIDDEN1, HIDDEN2 = 512, 256
TABLE_ROWS = [1250, 1000, 125000, 1250, 1000, 1000, 12500, 12500, 1000, 1250, 12500, 12500, 12500, 1250,
              12500, 12500, 1000, 12500, 1000, 1000, 1000, 1250, 1000, 1250, 1000, 1000, 1250]
P = 128
TILES = BATCH // P
SLOTS = 2
PAIRS_OF_TILES = TILES // SLOTS

ONE_HOT = 7
SMALL_ROWS = 1000
SMALL_P = 125
SMALL_K = SMALL_ROWS // SMALL_P
RAW = 3
SPLITS = 3
PARTS = 3
PIECES = 2
PIECE = SMALL_K // PIECES
ONE_HOT_FEATURES = [f for f in range(FEATURES) if TABLE_ROWS[f] == SMALL_ROWS][:ONE_HOT]

ORDER = ONE_HOT_FEATURES + [f for f in range(FEATURES) if f not in ONE_HOT_FEATURES]
FPC = 4
CHUNKS = [list(range(a, min(a + FPC, FEATURES))) for a in range(ONE_HOT, FEATURES, FPC)]
NC = len(CHUNKS)

WARM_UP = 20

QUADRANT = 32
PACK = P // QUADRANT
COLUMNS = FEATURES
GROUPS = -(-COLUMNS // PACK)
PPB = 4
NB = P // (PACK * PPB)
HALF_RING = 12
RING = 2 * HALF_RING
FIRST = HALF_RING // PACK
KEPT = GROUPS - FIRST
ROWS_USED = [max(RING, q + PACK * (GROUPS - 1)) if q + PACK * (GROUPS - 1) < COLUMNS else RING for q in range(PACK)]
ACROSS = (PACK - 1) * QUADRANT + max(ROWS_USED)
MERGES = {NB - 4: (0, NB - 4), NB - 2: (NB - 4, NB - 2), NB - 1: (NB - 2, NB)}
BANKS = 5
FIRST_BANK = NB % BANKS
COPIERS = 2
BEFORE_LAYER1 = NC // 2 + 1
N1 = HIDDEN1 // P
N2 = HIDDEN2 // P
NPB = N1 // 2
FIRST_HALF, SECOND_HALF = range(NPB), range(NPB, N1)

FILLED = COLUMNS % PACK * QUADRANT
STRIPS = [(q * QUADRANT + ROWS_USED[q], (q + 1) * QUADRANT, GROUPS if q * QUADRANT < FILLED else GROUPS - 1)
          for q in range(PACK)]
B_PLACES = ([(p, GROUPS - 1) for p in range(FILLED, P)]
            + [(p, g) for start, stop, end in STRIPS for p in range(start, stop) for g in range(FIRST, end)])
B_LOADS = 1 + len(STRIPS)
assert len(B_PLACES) >= DIM and FILLED == 3 * QUADRANT and RING == PACK * (GROUPS - 1)


def in_ring(g, r):
    ahead = (r - g) % RING
    return (g, True) if 1 <= ahead <= HALF_RING else (g - HALF_RING, ahead > 0)


def bank_of_chunk(c):
    return (FIRST_BANK + c) % BANKS


def last_product_before(c):
    return max(b for b in range(NB) if b % BANKS == bank_of_chunk(c))


def dlrm_tower(nc, bottom, ids, small_ids, tables, w_first, w_last, b1, w2, b2, w3, takes_other, out):
    fp32 = mybir.dt.float32
    bf16 = mybir.dt.bfloat16
    fp16 = mybir.dt.float16
    u32 = mybir.dt.uint32
    ALU = mybir.AluOpType
    ACT = mybir.ActivationFunctionType

    with ExitStack() as ctx:
        def sb(name, shape, dt=fp32):
            return ctx.enter_context(nc.sbuf_tensor(name, shape, dt))

        def ps(name, shape):
            return ctx.enter_context(nc.psum_tensor(name, shape, fp32))

        def sem(name):
            return ctx.enter_context(nc.semaphore(name))

        ids_sb = sb("ids_sb", [P, TILES * FEATURES], u32)
        small_ids_sb = sb("small_ids_sb", [P, ONE_HOT, BATCH], u32)
        small_ids16 = sb("small_ids16", [P, ONE_HOT, BATCH], fp16)
        small_iota_sb = sb("small_iota_sb", [P, SMALL_K])
        raw = [sb(f"raw{h}", [P, SMALL_K, DIM]) for h in range(RAW)]
        rest = sb("rest", [P, SMALL_K, DIM])
        part = [[sb(f"part{h}_{j}", [P, SMALL_K, DIM], bf16) for j in range(PARTS)] for h in range(SPLITS)]
        one_hot = [sb(f"one_hot{h}", [P, SMALL_K, BATCH], bf16) for h in range(SPLITS)]
        selected = sb("selected", [DIM, ONE_HOT, BATCH])
        rows = [sb(f"rows{k}", [P, FEATURES - ONE_HOT, DIM]) for k in range(SLOTS)]
        rowsT = [sb(f"rowsT{k}", [DIM, P, QUADRANT]) for k in range(SLOTS)]
        pairs = [sb(f"pairs{k}", [P, GROUPS, P]) for k in range(SLOTS)]
        ident = sb("ident", [P, P])
        takes_other_sb = sb("takes_other_sb", [P, FIRST], u32)
        takes_other_all = sb("takes_other_all", [P, FIRST, P], u32)
        wp = sb("wp", [P, KEPT, HIDDEN1])
        wl = sb("wl", [P, KEPT, HIDDEN1])
        w2_sb = sb("w2_sb", [P, N1, HIDDEN2])
        w3_sb = sb("w3_sb", [P, N2])
        b1_sb = sb("b1_sb", [P, N1])
        b2_sb = sb("b2_sb", [P, N2])
        h1 = sb("h1", [P, N1, P])
        h2 = sb("h2", [P, N2, P])
        y_sb = sb("y_sb", [1, BATCH])

        ps_work = [ps(f"ps_work{i}", [P, BATCH]) for i in range(BANKS)]
        ps_acc = [ps(f"ps_acc{i}", [P, BATCH]) for i in range(3)]
        ACC = len(ps_acc)
        L2_BANK = [0, 2]
        L3_BANK = 1

        ids_loaded = sem("ids_loaded")
        small_iota_ready = sem("small_iota_ready")
        small_ids_loaded = [sem(f"small_ids_loaded{h}") for h in range(2)]
        raw_loaded = [[sem(f"raw_loaded{b}_{h}") for h in range(PIECES)] for b in range(RAW)]
        takes_other_loaded = sem("takes_other_loaded")
        takes_other_ready = sem("takes_other_ready")
        weights_loaded = sem("weights_loaded")
        ident_zeroed = sem("ident_zeroed")
        ident_ready = sem("ident_ready")
        weights_summed = sem("weights_summed")
        ids16_ready = sem("ids16_ready")
        one_hot_ready = sem("one_hot_ready")
        part_ready = [sem(f"part_ready{j}") for j in range(PARTS)]
        rest_ready = sem("rest_ready")
        one_hot_used = sem("one_hot_used")
        selected_ready = sem("selected_ready")
        selected_placed = sem("selected_placed")
        gathered = [[sem(f"gathered{k}_{c}") for c in range(NC)] for k in range(SLOTS)]
        bottom_loaded = [sem(f"bottom_loaded{k}") for k in range(SLOTS)]
        rows_transposed = sem("rows_transposed")
        placed = [sem("placed_dve"), sem("placed_act")]
        products_done = sem("products_done")
        taken = [sem("taken_dve"), sem("taken_act")]
        may_merge = sem("may_merge")
        merged = sem("merged")
        slot_free = [sem(f"slot_free{k}") for k in range(SLOTS)]
        layer1_done = sem("layer1_done")
        layer2_done = sem("layer2_done")
        layer3_done = sem("layer3_done")
        h1_written = sem("h1_written")
        h2_written = sem("h2_written")
        y_written = sem("y_written")
        y_stored = sem("y_stored")

        WEIGHT_LOADS = 6

        PLACED = [len(range(e, NC, COPIERS)) for e in range(COPIERS)]

        def load_small(queue, x):
            table = tables[ONE_HOT_FEATURES[x]].rearrange("(p k) d -> p k d", k=SMALL_K)
            for h in range(PIECES):
                ks = slice(h * PIECE, (h + 1) * PIECE)
                queue.dma_start(raw[x % RAW][0:SMALL_P, ks, :], table[:, ks, :]).then_inc(raw_loaded[x % RAW][h], 16)

        def load_bottom(sp, k, samples):
            spots = [(slice(FILLED, P), GROUPS - 1, GROUPS)] + [
                (slice(start, stop), FIRST, end) for start, stop, end in STRIPS]
            for partitions, g0, g1 in spots:
                sp.dma_start(pairs[k][partitions, g0:g1, :],
                             bottom[partitions, g0 - FIRST:g1 - FIRST, samples]).then_inc(bottom_loaded[k], 16)

        def place_rows(engine_copy, k, c):
            entries = CHUNKS[c]
            return engine_copy(rowsT[k][:, :, entries[0]:entries[-1] + 1].rearrange("p s f -> p f s"),
                               ps_work[bank_of_chunk(c)][:, 0:len(entries) * P].rearrange("p (f s) -> p f s", s=P))

        def take_products(engine_copy, k, b, samples):
            src = ps_work[b % BANKS][:, 0:PPB * PACK * COLUMNS].rearrange("p (m s g) -> p m s g", m=PPB, s=PACK)
            first = b * PPB * PACK
            dst = pairs[k][:, :, first:first + PPB * PACK].rearrange("p g (m s) -> p m s g", s=PACK)
            last = None
            for s in samples:
                for q in range(PACK):
                    n = -(-(COLUMNS - q) // PACK)
                    last = engine_copy(
                        dst[q * QUADRANT:q * QUADRANT + ROWS_USED[q], :, s, 0:n],
                        src[s * QUADRANT:s * QUADRANT + ROWS_USED[q], :, s, q:q + (n - 1) * PACK + 1:PACK])
            return last

        block = ctx.enter_context(nc.Block())

        @block.sync
        def _(sp):
            sp.dma_start(ids_sb[:].rearrange("p (t f) -> p t f", f=FEATURES),
                         ids.rearrange("(t p) f -> p t f", p=P)).then_inc(ids_loaded, 16)
            sp.dma_start(small_ids_sb[:, 0:1, :], small_ids[0:1, :].partition_broadcast(P)).then_inc(small_ids_loaded[0], 16)
            sp.dma_start(small_ids_sb[:, 1:ONE_HOT, :], small_ids[1:ONE_HOT, :].partition_broadcast(P)
                         ).then_inc(small_ids_loaded[1], 16)
            for x in range(1, RAW):
                load_small(sp, x)
            for x in range(RAW, ONE_HOT):
                sp.wait_ge(rest_ready, (x - RAW + 1) * PIECES)
                load_small(sp, x)
            sp.dma_start(takes_other_sb[:], takes_other).then_inc(takes_other_loaded, 16)
            sp.dma_start(wp[:], w_first).then_inc(weights_loaded, 16)
            sp.dma_start(wl[:], w_last).then_inc(weights_loaded, 16)
            sp.dma_start(w2_sb[:], w2.rearrange("(k p) n -> p k n", p=P)).then_inc(weights_loaded, 16)
            sp.dma_start(b1_sb[:], b1).then_inc(weights_loaded, 16)
            sp.dma_start(b2_sb[:], b2).then_inc(weights_loaded, 16)
            sp.dma_start(w3_sb[:], w3).then_inc(weights_loaded, 16)
            for k in range(SLOTS):
                load_bottom(sp, k, slice(k * P, (k + 1) * P))
            with sp.Fori(0, PAIRS_OF_TILES - 1) as i:
                for k in range(SLOTS):
                    sp.wait_ge(slot_free[k], i + 2)
                    load_bottom(sp, k, bass.ds((i + 1) * (SLOTS * P) + k * P, P))
            sp.wait_ge(y_written, 1 + TILES)
            sp.dma_start(out, y_sb[:]).then_inc(y_stored, 16)
            sp.wait_ge(y_stored, 16)

        @block.gpsimd
        def _(pool):
            nc.gpsimd.memset(ident[:], 0.0).then_inc(ident_zeroed, 1)
            pool.wait_ge(ident_zeroed, 1)
            nc.gpsimd.affine_select(out=ident[:], in_=ident[:], compare_op=ALU.not_equal, fill=1.0, base=0,
                                    pattern=[[-1, P]], channel_multiplier=1).then_inc(ident_ready, 1)
            nc.gpsimd.iota(small_iota_sb[:], pattern=[[1, SMALL_K]], base=0, channel_multiplier=SMALL_K,
                           allow_small_or_imprecise_dtypes=True).then_inc(small_iota_ready, 1)
            pool.wait_ge(ids_loaded, 16)
            for t in range(TILES):
                i, k = divmod(t, SLOTS)
                for c, entries in enumerate(CHUNKS):
                    if i:
                        pool.wait_ge(rows_transposed, (t - SLOTS) * NC + c + 1)
                    for e in entries:
                        at = t * FEATURES + ORDER[e]
                        nc.gpsimd.indirect_dma_start(
                            out=rows[k][:, e - ONE_HOT, :], out_offset=None, in_=tables[ORDER[e]],
                            in_offset=bass.IndirectOffsetOnAxis(ap=ids_sb[:, at:at + 1], axis=0),
                        ).then_inc(gathered[k][c], 16)

        @block.tensor
        def _(pe):
            pe.wait_ge(ident_ready, 1)
            for _ in range(WARM_UP):
                nc.tensor.transpose(ps_work[0][:, 0:P], ident[:], ident[:])

            def transposes(i, k, chunks):
                for c in chunks:
                    pe.wait_ge(gathered[k][c], (i + 1) * (16 * len(CHUNKS[c])))
                    if c >= BANKS:
                        e = (c - BANKS) % COPIERS
                        pe.wait_ge(placed[e], (i * SLOTS + k) * PLACED[e] + (c - BANKS) // COPIERS + 1)
                    else:
                        for e in taken:
                            pe.wait_ge(e, (i * SLOTS + k) * NB + last_product_before(c) + 1)
                    for j, position in enumerate(CHUNKS[c]):
                        last = nc.tensor.transpose(ps_work[bank_of_chunk(c)][:, j * P:(j + 1) * P],
                                                   rows[k][:, position - ONE_HOT, :], ident[:])
                    last.then_inc(rows_transposed, 1)

            for x in range(ONE_HOT):
                if x == ONE_HOT - 1:
                    transposes(0, 0, range(NC))
                if x >= ACC:
                    pe.wait_ge(selected_ready, x - ACC + 1)
                for j in range(PARTS):
                    for r in range(SMALL_K):
                        if r % PIECE == 0:
                            pe.wait_ge(part_ready[j], x * PIECES + r // PIECE + 1)
                        if j == 0:
                            pe.wait_ge(one_hot_ready, x * SMALL_K + r + 1)
                        last = nc.tensor.matmul(
                            ps_acc[x % ACC][:], part[x % SPLITS][j][0:SMALL_P, r, :],
                            one_hot[x % SPLITS][0:SMALL_P, r, :],
                            start=j == 0 and r == 0, stop=j == PARTS - 1 and r == SMALL_K - 1)
                last.then_inc(one_hot_used, 1)

            def products(i, k):
                pe.wait_ge(selected_placed, i * SLOTS + k + 2)
                for e in range(COPIERS):
                    pe.wait_ge(placed[e], (i * SLOTS + k + 1) * PLACED[e])
                for b in range(NB):
                    if b >= BANKS:
                        for e in taken:
                            pe.wait_ge(e, (i * SLOTS + k + 1) * NB + b - BANKS + 1)
                    for m in range(PPB):
                        s0 = (b * PPB + m) * PACK
                        at = m * PACK * COLUMNS
                        last = nc.tensor.matmul(
                            ps_work[b % BANKS][0:ACROSS, at:at + PACK * COLUMNS].rearrange(
                                "p (s g) -> p s g", s=PACK),
                            rowsT[k][:, s0:s0 + PACK, :].rearrange("p s f -> p (s f)")[:, 0:ACROSS],
                            rowsT[k][:, s0:s0 + PACK, 0:FEATURES], start=True, stop=True)
                    last.then_inc(products_done, 1)

            def layer1(i, k, first=False):
                if first:
                    pe.wait_ge(weights_loaded, 16 * WEIGHT_LOADS)
                    pe.wait_ge(weights_summed, 1)
                    pe.wait_ge(selected_ready, ONE_HOT)
                pe.wait_ge(bottom_loaded[k], (i + 1) * (16 * B_LOADS))
                for e in taken:
                    pe.wait_ge(e, (i * SLOTS + k + 2) * NB)
                pe.wait_ge(merged, (i * SLOTS + k + 1) * len(MERGES))
                for n in range(N1):
                    if n == NPB:
                        pe.wait_ge(y_written, i * SLOTS + k + 1)
                    for g in range(FIRST, GROUPS):
                        last = nc.tensor.matmul(ps_acc[n // NPB][:, (n % NPB) * P:(n % NPB + 1) * P],
                                                wp[:, g - FIRST, n * P:(n + 1) * P], pairs[k][:, g, :],
                                                start=g == FIRST, stop=g == GROUPS - 1)
                    if n % NPB == NPB - 1:
                        last.then_inc(layer1_done, 1)

            def layer2(i, k, blocks):
                pe.wait_ge(h1_written, (i * SLOTS + k) * N1 + blocks[-1] + 1)
                for m in range(N2):
                    for n in blocks:
                        last = nc.tensor.matmul(ps_acc[L2_BANK[m]][:, 0:P], w2_sb[:, n, m * P:(m + 1) * P],
                                                h1[:, n, :], start=n == 0, stop=n == N1 - 1)
                    if blocks == SECOND_HALF:
                        last.then_inc(layer2_done, 1)
                    elif m == 0:
                        last.then_inc(slot_free[k], 1)

            def layer3(i, k):
                for m in range(N2):
                    pe.wait_ge(h2_written, (i * SLOTS + k) * N2 + m + 1)
                    last = nc.tensor.matmul(ps_acc[L3_BANK][0:1, 0:P], w3_sb[:, m:m + 1], h2[:, m, :],
                                            start=m == 0, stop=m == N2 - 1)
                last.then_inc(layer3_done, 1)

            def step(tile, before=None, after=None):
                products(*tile)
                if before:
                    layer2(*before, SECOND_HALF)
                if after:
                    transposes(*after, range(BEFORE_LAYER1))
                if before:
                    layer3(*before)
                layer1(*tile, first=before is None)
                if after:
                    transposes(*after, range(BEFORE_LAYER1, NC))
                layer2(*tile, FIRST_HALF)

            step((0, 0), after=(0, 1))
            with pe.Fori(0, PAIRS_OF_TILES - 1) as i:
                step((i, 1), before=(i, 0), after=(i + 1, 0))
                step((i + 1, 0), before=(i, 1), after=(i + 1, 1))
            final = (PAIRS_OF_TILES - 1, 1)
            step(final, before=(PAIRS_OF_TILES - 1, 0))
            layer2(*final, SECOND_HALF)
            layer3(*final)

        @block.vector
        def _(dve):
            for k in range(SLOTS):
                nc.vector.memset(pairs[k][:, 0:FIRST, :], 0.0)
                nc.vector.memset(rowsT[k][:, :, FEATURES:QUADRANT], 0.0).then_inc(slot_free[k], 1)
            for s in taken:
                dve.sem_inc(s, NB)
            dve.sem_inc(y_written, 1)
            dve.wait_ge(small_iota_ready, 1)
            for x in range(ONE_HOT):
                dve.wait_ge(small_ids_loaded[min(x, 1)], 16)
                nc.vector.tensor_copy(small_ids16[:, x, :], small_ids_sb[:, x, :]).then_inc(ids16_ready, 1)
                if x >= SPLITS:
                    dve.wait_ge(one_hot_used, x - SPLITS + 1)
                dve.wait_ge(ids16_ready, x + 1)
                for h in range(PIECES):
                    ks = slice(h * PIECE, (h + 1) * PIECE)
                    for r in range(h * PIECE, (h + 1) * PIECE):
                        nc.vector.tensor_scalar(one_hot[x % SPLITS][:, r, :], small_ids16[:, x, :],
                                                small_iota_sb[:, r:r + 1], None, ALU.is_equal).then_inc(one_hot_ready, 1)
                    dve.wait_ge(raw_loaded[x % RAW][h], 16 * (x // RAW + 1))
                    dve.wait_ge(part_ready[0], x * PIECES + h + 1)
                    if x >= 1:
                        dve.wait_ge(part_ready[2], (x - 1) * PIECES + h + 1)
                    nc.vector.tensor_tensor(rest[0:SMALL_P, ks], raw[x % RAW][0:SMALL_P, ks],
                                            part[x % SPLITS][0][0:SMALL_P, ks], ALU.subtract).then_inc(rest_ready, 1)
                for h in range(PIECES):
                    ks = slice(h * PIECE, (h + 1) * PIECE)
                    dve.wait_ge(part_ready[1], x * PIECES + h + 1)
                    nc.vector.tensor_tensor(part[x % SPLITS][2][0:SMALL_P, ks], rest[0:SMALL_P, ks],
                                            part[x % SPLITS][1][0:SMALL_P, ks], ALU.subtract).then_inc(part_ready[2], 1)
            dve.wait_ge(weights_loaded, 16 * WEIGHT_LOADS)
            nc.vector.tensor_tensor(wp[:], wp[:], wl[:], ALU.add).then_inc(weights_summed, 1)
            dve.wait_ge(takes_other_loaded, 16)
            nc.vector.tensor_copy(takes_other_all[:], takes_other_sb[:].unsqueeze(2).broadcast_to([P, FIRST, P])
                                  ).then_inc(takes_other_ready, 1)

            def merge(i, k, b):
                first, end = MERGES[b]
                samples = slice(first * PPB * PACK, end * PPB * PACK)
                for e in taken:
                    dve.wait_ge(e, (i * SLOTS + k + 1) * NB + end)
                dve.wait_ge(bottom_loaded[k], (i + 1) * (16 * B_LOADS))
                dve.sem_inc(may_merge, 1)
                dve.wait_ge(takes_other_ready, 1)
                nc.vector.copy_predicated(pairs[k][:, FIRST:2 * FIRST, samples], takes_other_all[:, :, samples],
                                          pairs[k][:, 0:FIRST, samples]).then_inc(merged, 1)

            with dve.Fori(0, PAIRS_OF_TILES) as i:
                for k in range(SLOTS):
                    dve.wait_ge(slot_free[k], i + 1)
                    for c in range(0, NC, COPIERS):
                        dve.wait_ge(rows_transposed, (i * SLOTS + k) * NC + c + 1)
                        place_rows(nc.vector.tensor_copy, k, c).then_inc(placed[0], 1)
                    for b in range(NB):
                        dve.wait_ge(products_done, (i * SLOTS + k) * NB + b + 1)
                        take_products(nc.vector.tensor_copy, k, b, range(PACK // 2, PACK)).then_inc(taken[0], 1)
                        if b in MERGES:
                            merge(i, k, b)

        @block.scalar
        def _(act):
            def first_part(x):
                if x >= SPLITS:
                    act.wait_ge(one_hot_used, x - SPLITS + 1)
                for h in range(PIECES):
                    ks = slice(h * PIECE, (h + 1) * PIECE)
                    act.wait_ge(raw_loaded[x % RAW][h], 16 * (x // RAW + 1))
                    nc.scalar.copy(part[x % SPLITS][0][0:SMALL_P, ks], raw[x % RAW][0:SMALL_P, ks]).then_inc(part_ready[0], 1)

            def copy_selected(x):
                act.wait_ge(one_hot_used, x + 1)
                nc.scalar.copy(selected[:, x, :], ps_acc[x % ACC][:]).then_inc(selected_ready, 1)

            def place_selected(i, k, tables_placed):
                nc.scalar.copy(rowsT[k][:, :, tables_placed].rearrange("p s f -> p f s"),
                               selected[:, tables_placed, bass.ds((i * SLOTS + k) * P, P)]).then_inc(selected_placed, 1)

            def place(i, k, chunks):
                for c in (c for c in chunks if c % COPIERS == 1):
                    act.wait_ge(rows_transposed, (i * SLOTS + k) * NC + c + 1)
                    place_rows(nc.scalar.copy, k, c).then_inc(placed[1], 1)

            load_small(act, 0)
            first_part(0)
            for x in range(ONE_HOT):
                for h in range(PIECES):
                    ks = slice(h * PIECE, (h + 1) * PIECE)
                    act.wait_ge(rest_ready, x * PIECES + h + 1)
                    nc.scalar.copy(part[x % SPLITS][1][0:SMALL_P, ks], rest[0:SMALL_P, ks]).then_inc(part_ready[1], 1)
                if x >= 1:
                    copy_selected(x - 1)
                if x + 1 < ONE_HOT:
                    first_part(x + 1)
            act.wait_ge(slot_free[0], 1)
            place(0, 0, range(NC))
            act.wait_ge(selected_ready, ONE_HOT - 1)
            place_selected(0, 0, slice(0, ONE_HOT - 1))
            act.wait_ge(one_hot_used, ONE_HOT)
            nc.scalar.copy(rowsT[0][:, :, ONE_HOT - 1], ps_acc[(ONE_HOT - 1) % ACC][:, 0:P]).then_inc(selected_placed, 1)
            copy_selected(ONE_HOT - 1)
            act.wait_ge(selected_ready, ONE_HOT)
            act.wait_ge(weights_loaded, 16 * WEIGHT_LOADS)

            def take(i, k):
                for b in range(NB):
                    act.wait_ge(products_done, (i * SLOTS + k) * NB + b + 1)
                    take_products(nc.scalar.copy, k, b, range(PACK // 2)).then_inc(taken[1], 1)

            def take_layer1(i, k):
                for n in range(N1):
                    if n % NPB == 0:
                        act.wait_ge(layer1_done, (i * SLOTS + k) * 2 + n // NPB + 1)
                    nc.scalar.activation(h1[:, n, :], ps_acc[n // NPB][:, (n % NPB) * P:(n % NPB + 1) * P],
                                         ACT.Relu, bias=b1_sb[:, n:n + 1]).then_inc(h1_written, 1)

            def take_layer2(i, k):
                for m in range(N2):
                    act.wait_ge(layer2_done, (i * SLOTS + k) * N2 + m + 1)
                    nc.scalar.activation(h2[:, m, :], ps_acc[L2_BANK[m]][:, 0:P], ACT.Relu,
                                         bias=b2_sb[:, m:m + 1]).then_inc(h2_written, 1)

            def take_layer3(i, k):
                act.wait_ge(layer3_done, i * SLOTS + k + 1)
                nc.scalar.copy(y_sb[0:1, bass.ds((i * SLOTS + k) * P, P)],
                               ps_acc[L3_BANK][0:1, 0:P]).then_inc(y_written, 1)

            def step(tile, before=None, after=None):
                take(*tile)
                if before:
                    take_layer2(*before)
                if after:
                    act.wait_ge(slot_free[after[1]], after[0] + 1)
                    place_selected(*after, slice(0, ONE_HOT))
                    place(*after, range(BEFORE_LAYER1))
                if before:
                    take_layer3(*before)
                take_layer1(*tile)
                if after:
                    place(*after, range(BEFORE_LAYER1, NC))

            step((0, 0), after=(0, 1))
            with act.Fori(0, PAIRS_OF_TILES - 1) as i:
                step((i, 1), before=(i, 0), after=(i + 1, 0))
                step((i + 1, 0), before=(i, 1), after=(i + 1, 1))
            final = (PAIRS_OF_TILES - 1, 1)
            step(final, before=(PAIRS_OF_TILES - 1, 0))
            take_layer2(*final)
            take_layer3(*final)


def kernel(**inputs):
    import numpy as np
    import concourse.bacc as bacc
    from concourse.bass_utils import run_bass_kernel_spmd

    w1 = np.asarray(inputs["W_top1"])
    w_first = np.zeros((P, KEPT, HIDDEN1), w1.dtype)
    w_last = np.zeros((P, KEPT, HIDDEN1), w1.dtype)
    takes_other = np.zeros((P, FIRST), np.uint32)
    for g in range(HALF_RING, FEATURES):
        group, q = divmod(g, PACK)
        for r in range(RING if g < RING else g):
            column, used = in_ring(g, r) if g < RING else (g, True)
            if used:
                lo, hi = sorted((ORDER[r], ORDER[column]))
                w_first[q * QUADRANT + r, group - FIRST] = w1[DIM + hi * (hi - 1) // 2 + lo]
            if column != g:
                takes_other[q * QUADRANT + r, group - FIRST] = 1
    bottom = np.zeros((P, KEPT, BATCH), np.float32)
    for d, (p, g) in zip(range(DIM), B_PLACES):
        w_first[p, g - FIRST] = w1[d]
        w_last[p, g - FIRST] = w1[d - DIM]
        bottom[p, g - FIRST] = np.asarray(inputs["r_bottom_mlp_out"])[:, d]
    ids = np.ascontiguousarray(inputs["ids"]).view(np.uint32)
    arrays = {
        "bottom": bottom,
        "ids": ids,
        "small_ids": ids[:, ONE_HOT_FEATURES].T,
        **{f"tbl_{f}": inputs[f"tbl_{f}"] for f in range(FEATURES)},
        "takes_other": takes_other,
        "w_first": w_first,
        "w_last": w_last,
        "b1": np.asarray(inputs["b_top1"]).reshape(N1, P).T,
        "w2": inputs["W_top2"],
        "b2": np.asarray(inputs["b_top2"]).reshape(N2, P).T,
        "w3": np.asarray(inputs["W_top3"]).reshape(N2, P).T,
    }
    arrays = {name: np.ascontiguousarray(a) for name, a in arrays.items()}

    nc = bacc.Bacc("TRN2", target_bir_lowering=False, num_devices=1)
    aps = {name: nc.dram_tensor(name, a.shape, mybir.dt.from_np(a.dtype), kind="ExternalInput").ap()
           for name, a in arrays.items()}
    out = nc.dram_tensor("out", (1, BATCH), mybir.dt.float32, kind="ExternalOutput").ap()
    dlrm_tower(nc, aps["bottom"], aps["ids"], aps["small_ids"],
               [aps[f"tbl_{f}"] for f in range(FEATURES)], aps["w_first"], aps["w_last"],
               aps["b1"], aps["w2"], aps["b2"], aps["w3"], aps["takes_other"], out)
    r = run_bass_kernel_spmd(nc, [arrays], core_ids=[0])
    return r.results[0]["out"].reshape(BATCH, 1)
```
